# Optimizing a Trainium2 kernel written in Bass

```python
import numpy as np
import jax
import jax.numpy as jnp

def _softmax(x, axis=-1):
    return jax.nn.softmax(x, axis=axis)

def _gelu(x):
    return jax.nn.gelu(x, approximate=True)

def _silu(x):
    return jax.nn.silu(x)

def _sigmoid(x):
    return jax.nn.sigmoid(x)

def _layernorm(x, axis=-1, eps=1e-05):
    m = jnp.mean(x, axis=axis, keepdims=True)
    v = jnp.var(x, axis=axis, keepdims=True)
    return (x - m) / jnp.sqrt(v + eps)

def _scatter_add(tgt, idx, src, axis=0):
    return tgt.at[idx].add(src)

def _segment_sum(src, seg, n):
    return jax.ops.segment_sum(src, seg, n)
kernel_name = 'mk_gnn_resnorm_d4_gnn_r32_8c0389'

def setup_inputs(seed: int=0):
    np.random.seed(seed)
    _w = jnp.asarray

    def _rec_inputs():
        import jax
        import jax.numpy as jnp
        _gk = jax.random.key(seed)
        x = -0.000202 + 1 * jax.random.normal(jax.random.fold_in(_gk, 1), (50000, 128), jnp.float32)
        src = jax.random.randint(jax.random.fold_in(_gk, 2), (25000,), 0, 50000, jnp.int32)
        dst = jax.random.randint(jax.random.fold_in(_gk, 3), (25000,), 0, 50000, jnp.int32)
        _o = jnp.argsort(dst, stable=True)
        src = src[_o]
        dst = dst[_o]
        edge_attr_128 = 9.41057e-06 + 1 * jax.random.normal(jax.random.fold_in(_gk, 12), (25000, 128), jnp.float32)
        edge_attr_6 = 0.00011001 + 1.00018 * jax.random.normal(jax.random.fold_in(_gk, 13), (25000, 6), jnp.float32)
        return (x, src, dst, edge_attr_128, edge_attr_6)
    x, src, dst, edge_attr_128, edge_attr_6 = _rec_inputs()

    def _L0_gnn_setup():
        import jax, jax.numpy as jnp
        import numpy as np
        N_NODES = 50000
        N_EDGES = 18750
        D = 128
        key = jax.random.key(seed)
        k1, k2, k3 = jax.random.split(key, 3)
        x = jax.random.normal(k1, (N_NODES, D), dtype=jnp.float32)
        edge_index = jax.random.randint(k2, (2, N_EDGES), 0, N_NODES, dtype=jnp.int32)
        weight = jax.random.normal(k3, (D, D), dtype=jnp.float32) / np.sqrt(D)
        bias = jnp.zeros((D,), dtype=jnp.float32)
        return {'x': x, 'edge_index': edge_index, 'weight': weight, 'bias': bias}
    _L0_gnn_all = _L0_gnn_setup()
    _L0_gnn_in = {k: v for k, v in _L0_gnn_all.items() if k in ('weight', 'bias')}
    del _L0_gnn_all

    def _L1_gnn_setup():
        import jax, jax.numpy as jnp
        import numpy as np
        N, E, B = (3125, 50000, 16)
        NODE_IN, EDGE_OUT, GLOBAL_IN, NODE_OUT, HID = (128, 128, 64, 128, 128)

        def _glorot(key, shape):
            fan_in, fan_out = shape
            lim = np.sqrt(6.0 / (fan_in + fan_out)).astype(np.float32)
            return jax.random.uniform(key, shape, jnp.float32, -lim, lim)
        key = jax.random.key(seed)
        ks = jax.random.split(key, 12)
        return {'x': jax.random.normal(ks[0], (N, NODE_IN), jnp.float32), 'edge_index': jax.random.randint(ks[1], (2, E), 0, N, jnp.int64), 'edge_attr': jax.random.normal(ks[2], (E, EDGE_OUT), jnp.float32), 'u': jax.random.normal(ks[3], (B, GLOBAL_IN), jnp.float32), 'batch': jax.random.randint(ks[4], (N,), 0, B, jnp.int64), 'W1a': _glorot(ks[5], (NODE_IN + EDGE_OUT, HID)), 'b1a': jnp.zeros((HID,), jnp.float32), 'W1b': _glorot(ks[6], (HID, HID)), 'b1b': jnp.zeros((HID,), jnp.float32), 'W2a': _glorot(ks[7], (NODE_IN + HID + GLOBAL_IN, HID)), 'b2a': jnp.zeros((HID,), jnp.float32), 'W2b': _glorot(ks[8], (HID, NODE_OUT)), 'b2b': jnp.zeros((NODE_OUT,), jnp.float32)}
    _L1_gnn_all = _L1_gnn_setup()
    _L1_gnn_in = {k: v for k, v in _L1_gnn_all.items() if k in ('u', 'W1a', 'b1a', 'W1b', 'b1b', 'W2a', 'b2a', 'W2b', 'b2b')}
    del _L1_gnn_all

    def _L2_gnn_setup():
        import jax, jax.numpy as jnp
        import numpy as np
        N_NODES = 3125
        N_EDGES = 18750
        D_FEAT = 128
        key = jax.random.key(seed)
        k1, k2 = jax.random.split(key)
        node_features = jax.random.normal(k1, (N_NODES, D_FEAT), dtype=jnp.float32)
        edge_index = jax.random.randint(k2, (2, N_EDGES), 0, N_NODES, dtype=jnp.int64)
        learned_weight = jnp.array([0.8], dtype=jnp.float32)
        return {'node_features': node_features, 'edge_index': edge_index, 'learned_weight': learned_weight}
    _L2_gnn_all = _L2_gnn_setup()
    _L2_gnn_in = {k: v for k, v in _L2_gnn_all.items() if k in ('learned_weight',)}
    del _L2_gnn_all

    def _L3_gnn_setup():
        import jax, jax.numpy as jnp
        import numpy as np
        N_NODES = 50000
        N_EDGES = 25000
        IN_F = 128
        OUT_F = 128
        EDGE_F = 6
        key = jax.random.key(seed)
        k1, k2, k3, k4, k5, k6, k7 = jax.random.split(key, 7)
        nodeFeatures = jax.random.normal(k1, (N_NODES, IN_F), dtype=jnp.float32)
        edgeIndex = jax.random.randint(k2, (N_EDGES, 2), 0, N_NODES, dtype=jnp.int64)
        edgeFeatures = jax.random.normal(k3, (N_EDGES, EDGE_F), dtype=jnp.float32)
        lim_n = 1.0 / np.sqrt(IN_F)
        lim_e = 1.0 / np.sqrt(EDGE_F)
        W = jax.random.uniform(k4, (IN_F, OUT_F), minval=-lim_n, maxval=lim_n, dtype=jnp.float32)
        b = jax.random.uniform(k5, (OUT_F,), minval=-lim_n, maxval=lim_n, dtype=jnp.float32)
        We = jax.random.uniform(k6, (EDGE_F, OUT_F), minval=-lim_e, maxval=lim_e, dtype=jnp.float32)
        be = jax.random.uniform(k7, (OUT_F,), minval=-lim_e, maxval=lim_e, dtype=jnp.float32)
        return {'nodeFeatures': nodeFeatures, 'edgeIndex': edgeIndex, 'edgeFeatures': edgeFeatures, 'W': W, 'b': b, 'We': We, 'be': be}
    _L3_gnn_all = _L3_gnn_setup()
    _L3_gnn_in = {k: v for k, v in _L3_gnn_all.items() if k in ('W', 'b', 'We', 'be')}
    del _L3_gnn_all
    return {'x': x, 'src': src, 'dst': dst, 'edge_attr_128': edge_attr_128, 'edge_attr_6': edge_attr_6, 'L0_gnn_weight': _L0_gnn_in['weight'], 'L0_gnn_bias': _L0_gnn_in['bias'], 'L1_gnn_u': _L1_gnn_in['u'], 'L1_gnn_W1a': _L1_gnn_in['W1a'], 'L1_gnn_b1a': _L1_gnn_in['b1a'], 'L1_gnn_W1b': _L1_gnn_in['W1b'], 'L1_gnn_b1b': _L1_gnn_in['b1b'], 'L1_gnn_W2a': _L1_gnn_in['W2a'], 'L1_gnn_b2a': _L1_gnn_in['b2a'], 'L1_gnn_W2b': _L1_gnn_in['W2b'], 'L1_gnn_b2b': _L1_gnn_in['b2b'], 'L2_gnn_learned_weight': _L2_gnn_in['learned_weight'], 'L3_gnn_W': _L3_gnn_in['W'], 'L3_gnn_b': _L3_gnn_in['b'], 'L3_gnn_We': _L3_gnn_in['We'], 'L3_gnn_be': _L3_gnn_in['be']}

def reference(x, src, dst, edge_attr_128, edge_attr_6, L0_gnn_weight, L0_gnn_bias, L1_gnn_u, L1_gnn_W1a, L1_gnn_b1a, L1_gnn_W1b, L1_gnn_b1b, L1_gnn_W2a, L1_gnn_b2a, L1_gnn_W2b, L1_gnn_b2b, L2_gnn_learned_weight, L3_gnn_W, L3_gnn_b, L3_gnn_We, L3_gnn_be):
    import jax
    import jax.numpy as jnp

    def _L0_gnn_ref(x, edge_index, weight, bias):
        import jax, jax.numpy as jnp
        import numpy as np
        N_NODES = 50000
        N_EDGES = 18750
        D = 128
        n = x.shape[0]
        src, dst = (edge_index[0], edge_index[1])
        loop = jnp.arange(n, dtype=src.dtype)
        src = jnp.concatenate([src, loop])
        dst = jnp.concatenate([dst, loop])
        deg = jax.ops.segment_sum(jnp.ones_like(dst, dtype=x.dtype), dst, num_segments=n)
        dinv = jnp.where(deg > 0, jax.lax.rsqrt(deg), jnp.zeros_like(deg))
        norm = dinv[src] * dinv[dst]
        xw = x @ weight
        out = jax.ops.segment_sum(norm[:, None] * xw[src], dst, num_segments=n)
        out = out + bias
        return jax.nn.relu(out)

    def _L1_gnn_ref(x, edge_index, edge_attr, u, batch, W1a, b1a, W1b, b1b, W2a, b2a, W2b, b2b):
        import jax, jax.numpy as jnp
        import numpy as np
        N, E, B = (3125, 50000, 16)
        NODE_IN, EDGE_OUT, GLOBAL_IN, NODE_OUT, HID = (128, 128, 64, 128, 128)

        def _glorot(key, shape):
            fan_in, fan_out = shape
            lim = np.sqrt(6.0 / (fan_in + fan_out)).astype(np.float32)
            return jax.random.uniform(key, shape, jnp.float32, -lim, lim)
        row, col = (edge_index[0], edge_index[1])
        h = jnp.concatenate([x[row], edge_attr], axis=1)
        h = jax.nn.relu(h @ W1a + b1a) @ W1b + b1b
        summed = jax.ops.segment_sum(h, col, num_segments=x.shape[0])
        cnt = jax.ops.segment_sum(jnp.ones((h.shape[0],), h.dtype), col, num_segments=x.shape[0])
        agg = summed / jnp.clip(cnt, 1.0)[:, None]
        z = jnp.concatenate([x, agg, u[batch]], axis=1)
        return jax.nn.relu(z @ W2a + b2a) @ W2b + b2b

    def _L2_gnn_ref(node_features, edge_index, learned_weight):
        import jax, jax.numpy as jnp
        import numpy as np
        N_NODES = 3125
        N_EDGES = 18750
        D_FEAT = 128
        src, dst = (edge_index[0], edge_index[1])
        messages = node_features[src] * learned_weight
        out = jnp.zeros_like(node_features).at[dst].add(messages)
        return out

    def _L3_gnn_ref(nodeFeatures, edgeIndex, edgeFeatures, W, b, We, be):
        import jax, jax.numpy as jnp
        import numpy as np
        N_NODES = 50000
        N_EDGES = 25000
        IN_F = 128
        OUT_F = 128
        EDGE_F = 6
        transformed = nodeFeatures @ W + b
        edgeMsg = edgeFeatures @ We + be
        src = edgeIndex[:, 0]
        dst = edgeIndex[:, 1]
        messages = transformed[src] + edgeMsg
        aggregated = jax.ops.segment_sum(messages, dst, num_segments=nodeFeatures.shape[0])
        return jax.nn.relu(aggregated)
    edge_index = jnp.stack([src, dst])
    edge_index_t = jnp.stack([src, dst], axis=1)
    batch0 = jnp.zeros((50000,), jnp.int32)
    x = _layernorm(x + _L0_gnn_ref(x, edge_index, L0_gnn_weight, L0_gnn_bias), axis=-1)
    x = _layernorm(x + _L1_gnn_ref(x, edge_index, edge_attr_128, L1_gnn_u, batch0, L1_gnn_W1a, L1_gnn_b1a, L1_gnn_W1b, L1_gnn_b1b, L1_gnn_W2a, L1_gnn_b2a, L1_gnn_W2b, L1_gnn_b2b), axis=-1)
    x = _layernorm(x + _L2_gnn_ref(x, edge_index, L2_gnn_learned_weight), axis=-1)
    x = _layernorm(x + _L3_gnn_ref(x, edge_index_t, edge_attr_6, L3_gnn_W, L3_gnn_b, L3_gnn_We, L3_gnn_be), axis=-1)
    return x

_drawn_inputs = setup_inputs


def setup_inputs(seed=0):
    import zlib

    import numpy as np

    out = dict(_drawn_inputs(seed))
    spreads = {'L0_gnn_bias': (0.0, 0.1),
     'L1_gnn_b1a': (0.0, 0.57),
     'L1_gnn_b1b': (0.0, 0.369),
     'L1_gnn_b2a': (0.0, 0.1),
     'L1_gnn_b2b': (0.0, 0.1)}
    factors = {}
    for name, (base, spread) in spreads.items():
        noise = np.random.default_rng([zlib.crc32(name.encode()), seed]).standard_normal(out[name].shape)
        drawn = base * np.exp(spread * noise) if base else spread * noise
        out[name] = jnp.asarray(drawn.astype(out[name].dtype))
    for name, factor in factors.items():
        out[name] = (out[name] * factor).astype(out[name].dtype)
    return out
```

```python
from contextlib import ExitStack

import concourse.bass as bass
from concourse import mybir

F32 = mybir.dt.float32
F16 = mybir.dt.float16
BF16 = mybir.dt.bfloat16
I32 = mybir.dt.int32
ALU = mybir.AluOpType
ACT = mybir.ActivationFunctionType
AX_X = mybir.AxisListType.X

P = 128
D = 128
EPS = 1e-5
GROUP = 4
GATHERS_IN_FLIGHT = 8
LAYERS = 4
RING = 4
SLOTS = 6
ACT_HOTS = 3
HOTS = 3
LEAD = 4
HOTS_POOL = {0: 3, 3: 2}
NORM_LAG = [5, 5, 3, 3]


class Step:

    def __init__(self, g, slot, turn, slots):
        self.g, self.slot, self.turn, self.slots = g, slot, turn, slots

    def back(self, n):
        slot = self.slot - n
        return Step(self.g - n, slot % self.slots, self.turn + slot // self.slots, self.slots)


def walk(eng, count, slots, head, step, tail, rounds=2):
    unrolled = rounds * slots
    turns = (count - head) // unrolled
    assert head + turns * unrolled == count and turns >= 1
    for g in range(head):
        step(Step(g, g % slots, g // slots, slots), False)
    with eng.Fori(0, turns) as i:
        for u in range(unrolled):
            at = head + u
            step(Step(i * unrolled + at, at % slots, i * rounds + at // slots, slots), False)
    for g in range(count, count + tail):
        step(Step(g, g % slots, g // slots, slots), True)


def walk_pairs(eng, start, stop, count, tail, step):
    assert (stop - start) % SLOTS == 0
    for i in range(start):
        step(Step(i, i % SLOTS, i // SLOTS, SLOTS), False)
    with eng.Fori(0, (stop - start) // SLOTS) as k:
        for u in range(start, start + SLOTS):
            step(Step(k * SLOTS + u, u % SLOTS, k + u // SLOTS, SLOTS), False)
    for i in range(stop, count + tail):
        step(Step(i, i % SLOTS, i // SLOTS, SLOTS), i >= count)


def both(p):
    for k in range(2):
        slot = 2 * p.slot + k
        yield Step(p.g * 2 + k, slot % SLOTS, p.turn * 2 + slot // SLOTS, SLOTS)


def ahead(p, n):
    return p.back(-n)


def past(g, n):
    return not isinstance(g, int) or g >= n


def over(ap, n):
    return ap.unsqueeze(1).to_broadcast([ap.shape[0], n, ap.shape[1]])


def along(ap, n):
    return ap.unsqueeze(2).to_broadcast([ap.shape[0], ap.shape[1], n])


def build(nc, x, src, dst, edge_attr_128, edge_attr_6, w0, bias0, u, w1a, b1a, w1b, b1b, w2a, b2a,
          w2b, b2b, learned, w3, b3, we, be, out):
    N = x.shape[0]
    E = src.shape[0]
    EF = edge_attr_6.shape[1]
    UF = u.shape[1]
    NT = -(-N // (P * GROUP)) * GROUP
    NG = NT // GROUP
    ET = -(-E // P)
    EG = ET // GROUP
    assert ET % GROUP == 0 and ET > P and (NG - 2) % SLOTS == 0 and EG % 2 == 1
    QT = NT // 4
    E_LAST = E - (ET - 1) * P
    ROWS1 = ET - P
    GR = GROUP * P
    LAST_ROWS = N - (NG - 1) * GR
    LAST_FULL, LAST_PART = LAST_ROWS // P, LAST_ROWS % P

    with ExitStack() as ctx:
        def sb(name, shape, dt=F32):
            return ctx.enter_context(nc.sbuf_tensor(name, shape, dt))

        def sem(name):
            return ctx.enter_context(nc.semaphore(name))

        def dram(name, shape):
            return nc.dram_tensor(name, shape, F32, kind="Internal").ap()

        x_rows = [x] + [dram(f"x_after_{n}", [NT * P, D]) for n in range(LAYERS - 1)] + [out]
        dst_rows_dram = dram("dst_rows_dram", [ET, P])

        messages = sb("messages", [P, ET + 1, D])
        src_index = sb("src_index", [P, ET], I32)
        dst_cols = sb("dst_cols", [P, ET + 1])
        src_weight = sb("src_weight", [P, ET + 1])
        iota = sb("iota", [P, P])
        base = sb("base", [P, NT])
        ident = sb("ident", [P, P])
        eps = sb("eps", [P, 1])
        dinv = sb("dinv", [P, NT])
        dinv_sq = sb("dinv_sq", [P, NT])
        rcount = sb("rcount", [P, NT])
        first_row = sb("first_row", [1, NT], I32)
        width = sb("width", [1, 1], I32)
        near = sb("near", [1, 1], I32)
        clamp = sb("clamp", [1, 2 * ET], I32)
        dst_rel = sb("dst_rel", [P, 2, NT])
        bias0_parts = sb("bias0_parts", [P, GROUP, D], BF16)
        ones_b = sb("ones_b", [P, P], BF16)
        rel_here = sb("rel_here", [P, SLOTS, GROUP])
        extra_hot = sb("extra_hot", [P, P])
        extra_rel = sb("extra_rel", [P, 1])
        rows_in = sb("rows_in", [P, SLOTS, GROUP, D])
        rows_sum = sb("rows_sum", [P, SLOTS, GROUP, D])
        stats = sb("stats", [P, 2, GROUP, 6])
        moments = sb("moments", [P, SLOTS, GROUP, 2])
        scale = sb("scale", [P, SLOTS, GROUP, 3])
        attr6 = sb("attr6", [P, SLOTS, GROUP, EF])
        w0_s = sb("w0_s", [P, D])
        w1a_s = sb("w1a_s", [P, 2, D])
        w2ax_s = sb("w2ax_s", [P, D])
        w2b_s = sb("w2b_s", [P, D])
        w1m = sb("w1m", [P, D])
        w3_s = sb("w3_s", [P, D])
        we_s = sb("we_s", [EF, D])
        bias_cols = sb("bias_cols", [P, 4])
        bias_all = sb("bias_all", [P, 4, D])
        b1m_all = sb("b1m_all", [P, D])
        learned_all = sb("learned_all", [P, 1])
        BIAS0, B2B, B3E = 0, 1, 2

        ARENA = 11264
        arena = sb("arena", [P, ARENA])
        onehots = arena[:, 0:HOTS * 1024].rearrange("p (b n d) -> p b n d", b=HOTS, d=P)
        rows_pool = arena[:, 8192:11264].rearrange("p (s t d) -> p s t d", s=SLOTS, d=D)
        rows_mid = arena[:, 3072:4096].rearrange("p (b t d) -> p b t d", b=2, d=D)
        rows_scaled = arena[:, 4096:5120].rearrange("p (b t d) -> p b t d", b=2, d=D)
        turned = arena[:, 5120:6144].rearrange("p (b n) -> p b n", b=2)
        turned2 = arena[:, 6144:7168].rearrange("p (b n) -> p b n", b=2)
        attr_turned = arena[:, 7168:8192].rearrange("p (b n) -> p b n", b=2)
        attr = arena[:, 0:3072].rearrange("p (s t d) -> p s t d", s=SLOTS, d=D)
        gathered_rows = {1: rows_sum, 3: rows_pool}
        windows = rows_sum[:, 0:2, :, :]
        used = [0]

        def early(shape, dt=F32):
            size = 1
            for n in shape:
                size *= n
            words = -(-size * (2 if dt == F16 else 4) // 4)
            at = used[0]
            used[0] += words
            assert used[0] <= ARENA
            piece = arena[:, at:at + words]
            if dt != F32:
                piece = piece.bitcast(dt)
            if len(shape) == 2:
                piece = piece.rearrange("p (a b) -> p a b", a=shape[0])
            if len(shape) == 3:
                piece = piece.rearrange("p (a b c) -> p a b c", a=shape[0], b=shape[1])
            return piece

        edge_rows_i = early([4, P], I32)
        edge_rows = early([4, P])
        split_i = early([4, ET], I32)
        split = early([4, ET])
        SRC_TILE, SRC_PLACE, DST_TILE, DST_PLACE = range(4)
        dst_index = early([ET], I32)
        src_count = early([ET])
        iota16 = early([P], F16)
        tile16 = early([NT], F16)
        edge_up = early([ET])
        edge_down = early([ET])
        part = early([1])
        ident16 = early([P], F16)
        ones = early([P])
        ones16 = early([2], F16)
        place_hot = early([RING, P], F16)
        tile_hot = early([RING, NT], F16)
        place_hot_t = early([RING, P], F16)
        picked = early([2, NT], F16)
        distance = early([ACT_HOTS, P], F16)
        count = early([NT])
        count_i = early([NT], I32)
        count_low_f = early([NT])
        count16 = early([3, NT], F16)
        span = early([2, 4])
        first_f = early([4, 4])
        widest = early([1])
        first_i = early([2, 4], I32)
        width_f = early([1])
        reach = early([NT])
        clamp_f = early([2 * ET])
        on_part = early([1])
        part_b = early([P // 2]).bitcast(BF16)
        spare = rows_in[:, :, :, :].rearrange("p s t d -> p (s t) d")
        present = rows_in[:, :, :, :].rearrange("p s t d -> p (s t d)")[:, 0:4 * ET].rearrange("p (c j) -> p c j", c=4)
        w1b_s, w1b_t, w2am_s, b1b_wide = (spare[:, n, :] for n in range(8, 12))
        w2au_s = spare[0:UF, 12, :]
        parts_f = spare[:, 13:16, :]
        u_col = early([1])[0:UF, :]
        bias_row = early([4, D])[0:1, :, :]

        bank = [ctx.enter_context(nc.psum_tensor(f"bank{n}", [P, 512], F32)) for n in range(8)]
        turned16 = [bank[n][:, :].bitcast(F16)[:, 0:P] for n in (6, 7)]
        turning = [bank[2], bank[3]]
        product = [bank[4], bank[5]]
        update = [bank[6], bank[7]]

        def tiled(b):
            return b[:, :].rearrange("p (t d) -> p t d", t=GROUP)

        summed = [tiled(bank[n]) for n in range(SLOTS)]
        SUM_BANKS = [2, 2, SLOTS, 3]

        pads_set = sem("pads_set")
        edges_loaded = sem("edges_loaded")
        weights_loaded = sem("weights_loaded")
        rows_cast = sem("rows_cast")
        edges_turned = sem("edges_turned")
        index_ready = sem("index_ready")
        iotas_ready = sem("iotas_ready")
        idents_ready = sem("idents_ready")
        hot_ready = sem("hot_ready")
        hist_done = sem("hist_done")
        count_ready = sem("count_ready")
        count16_ready = sem("count16_ready")
        roots_ready = sem("roots_ready")
        count_root = sem("count_root")
        prologue_step = sem("prologue_step")
        span_ready = sem("span_ready")
        span_turned = sem("span_turned")
        first_ready = sem("first_ready")
        near_ready = sem("near_ready")
        src_hot_ready = sem("src_hot_ready")
        src_hot_turned = sem("src_hot_turned")
        src_hot_copied = sem("src_hot_copied")
        src_picked = sem("src_picked")
        src_counted = sem("src_counted")
        src_root = sem("src_root")
        src_weight_ready = sem("src_weight_ready")
        dst_rows_stored = sem("dst_rows_stored")
        windows_gathered = sem("windows_gathered")
        windows_turned = sem("windows_turned")
        tables_ready = sem("tables_ready")
        fold_turned = sem("fold_turned")
        fold_copied = sem("fold_copied")
        folded = sem("folded")
        folds_copied = sem("folds_copied")
        src_distance = sem("src_distance")
        src_hot_dve = sem("src_hot_dve")
        biases_ready = sem("biases_ready")
        gather_landed = [sem(f"gather_landed{n}") for n in range(GATHERS_IN_FLIGHT)]
        gathered = sem("gathered")
        tail_loaded = sem("tail_loaded")
        tail_stored = sem("tail_stored")

        def per_layer(name, layers=range(LAYERS)):
            return {n: sem(f"l{n}_{name}") for n in layers}


        loaded = [sem(f"loaded{s}") for s in range(SLOTS)]
        stored = [sem(f"stored{s}") for s in range(SLOTS)]
        hots_ready = per_layer("hots_ready")
        sums_done = per_layer("sums_done")
        extra_step = per_layer("extra_step")
        extra_ready = per_layer("extra_ready")
        extra_used = per_layer("extra_used")
        mid_ready = per_layer("mid_ready", [0, 1])
        pool_ready = per_layer("pool_ready", [0, 1])
        turn_done = per_layer("turn_done", [0, 1])
        turn_copied = per_layer("turn_copied", [0, 1])
        product_done = per_layer("product_done", [0, 1])
        scaled_ready = per_layer("scaled_ready", [0, 1])
        hidden_turned = sem("l1_hidden_turned")
        hidden_copied = sem("l1_hidden_copied")
        update_done = sem("l1_update_done")
        learned_scaled = sem("l2_learned_scaled")
        own_scaled = sem("own_scaled")
        hots_pool = per_layer("hots_pool", HOTS_POOL)
        rel_copied = per_layer("rel_copied", HOTS_POOL)
        sum_ready = per_layer("sum_ready", [0, 1, 3])
        stats_done = per_layer("stats_done")
        moments_done = per_layer("moments_done")
        std_done = per_layer("std_done")
        inv_done = per_layer("inv_done")
        scale_done = per_layer("scale_done")
        normed = per_layer("normed")
        EDGE = [1, 3]
        attr_loaded = [sem(f"attr_loaded{s}") for s in range(SLOTS)]
        attr_tail = sem("attr_tail")
        e_turned = per_layer("e_turned", EDGE)
        e_copied_x = per_layer("e_copied_x", EDGE)
        e_copied_a = per_layer("e_copied_a", EDGE)
        e_hidden = sem("l1_e_hidden")
        e_relu = sem("l1_e_relu")
        e_product = per_layer("e_product", EDGE)
        messages_ready = per_layer("messages_ready", EDGE)

        def rows_here(eng, n, s):
            eng.wait_ge(loaded[s.slot], 16 * (n * len(range(s.slot, NG, SLOTS)) + s.turn + 1))

        def rows_out(eng, n, slot, turns):
            eng.wait_ge(stored[slot], 16 * (n * len(range(slot, NG, SLOTS)) + turns))

        def raw_free(eng, n, e):
            if past(e, SLOTS):
                eng.wait_ge(e_turned[n], e - (SLOTS - 1))

        def hots_of(eng, s, tiles):
            if tiles == 2 * GROUP:
                rel = dst_rel[:, :, bass.ds(s.g * GROUP, GROUP)]
                shape = [P, 2, GROUP, P]
                return eng.tensor_tensor(onehots[:, s.slot % HOTS, :, :].rearrange("p (k t) d -> p k t d", k=2),
                                         iota[:, :].unsqueeze(1).unsqueeze(1).to_broadcast(shape),
                                         rel.unsqueeze(3).to_broadcast(shape), ALU.is_equal)
            ins = eng.tensor_tensor(onehots[:, s.slot % HOTS, 0:GROUP, :], over(iota[:, :], GROUP),
                                    along(dst_rel[:, 0, bass.ds(s.g * GROUP, GROUP)], P), ALU.is_equal)
            if tiles > GROUP:
                ins = eng.tensor_tensor(onehots[:, s.slot % HOTS, GROUP:tiles, :], over(iota[:, :], tiles - GROUP),
                                        along(dst_rel[:, 1, bass.ds(s.g * GROUP, tiles - GROUP)], P), ALU.is_equal)
            return ins

        def there(e):
            return not isinstance(e.g, int) or e.g < EG

        def inside(q):
            return past(q.g, 0) and (not isinstance(q.g, int) or q.g < ET)

        def here(q):
            return past(q.g, 0) and (not isinstance(q.g, int) or q.g < NG)

        def all_stored(eng, n):
            for s in range(SLOTS):
                rows_out(eng, n, s, len(range(s, NG, SLOTS)))

        mats = [(w0_s[:, :], w0), (w1a_s[:, 0, :], w1a[0:D, :]), (w1a_s[:, 1, :], w1a[D:2 * D, :]),
                (w1b_s, w1b), (w2ax_s[:, :], w2a[0:D, :]), (w2am_s, w2a[D:2 * D, :]),
                (w2au_s, w2a[2 * D:2 * D + UF, :]), (w2b_s[:, :], w2b), (w3_s[:, :], w3),
                (we_s[:, :], we), (u_col, u[0:1, :].rearrange("a f -> f a"))]
        mats += [(bias_cols[:, n:n + 1], b.rearrange("(f a) -> f a", a=1)) for n, b in enumerate((b1a, b1b, b2a))]
        mats += [(bias_row[:, n, :], b.rearrange("(a f) -> a f", a=1)) for n, b in enumerate((bias0, b2b, b3, be))]
        mats += [(learned_all[:, :], learned.rearrange("(a f) -> a f", a=1).to_broadcast([P, 1]))]

        block = ctx.enter_context(nc.Block())

        @block.sync
        def _(sp):
            sp.wait_ge(pads_set, 1)
            for c, ids in ((0, src), (2, dst)):
                whole = ids[0:(ET - 1) * P].rearrange("(r p) -> r p", p=P)
                sp.dma_start(edge_rows_i[:, c, :], whole[0:P, :]).then_inc(edges_loaded, 16)
                sp.dma_start(edge_rows_i[0:ROWS1 - 1, c + 1, :], whole[P:ET - 1, :]).then_inc(edges_loaded, 16)
                sp.dma_start(edge_rows_i[ROWS1 - 1:ROWS1, c + 1, 0:E_LAST],
                             ids[(ET - 1) * P:E].rearrange("(r p) -> r p", r=1)).then_inc(edges_loaded, 16)
            for to, what in mats:
                sp.dma_start(to, what).then_inc(weights_loaded, 16)
            sp.wait_ge(rows_cast, 1)
            sp.dma_start(dst_rows_dram[0:P, :], edge_rows[:, 2, :]).then_inc(dst_rows_stored, 16)
            sp.dma_start(dst_rows_dram[P:ET, :], edge_rows[0:ROWS1, 3, :]).then_inc(dst_rows_stored, 16)
            def pick(rows, g):
                return rows[g] if isinstance(g, int) else rows[bass.ds(g, 1)].rearrange("a p t d -> p (a t) d")

            sp.wait_ge(tables_ready, 1)
            for n in range(LAYERS):
                if n > 0:
                    all_stored(sp, n - 1)
                if n in EDGE:
                    whose, to = (edge_attr_128, attr) if n == 1 else (edge_attr_6, attr6)
                    attr_groups = whose[0:(EG - 1) * GR, :].rearrange("(g t p) f -> g p t f", t=GROUP, p=P)

                    def load_attr(e, drain):
                        raw_free(sp, n, e.g)
                        if isinstance(e.g, int) and e.g == EG - 1:
                            e0 = (EG - 1) * GR
                            sp.dma_start(to[:, e.slot, 0:GROUP - 1, :],
                                         whose[e0:e0 + (GROUP - 1) * P, :].rearrange("(t p) f -> p t f", p=P)).then_inc(attr_tail, 16)
                            sp.wait_ge(attr_tail, 16 * (EDGE.index(n) + 1))
                            sp.dma_start(to[0:E_LAST, e.slot, GROUP - 1, :], whose[e0 + (GROUP - 1) * P:E, :])\
                                .then_inc(attr_loaded[e.slot], 16)
                        else:
                            sp.dma_start(to[:, e.slot, :, :], pick(attr_groups, e.g)).then_inc(attr_loaded[e.slot], 16)

                    def all_attrs():
                        for g in range(SLOTS):
                            load_attr(Step(g, g, 0, SLOTS), False)
                        turns = (EG - 1 - SLOTS) // SLOTS
                        with sp.Fori(0, turns) as i:
                            for v in range(SLOTS):
                                load_attr(Step((i + 1) * SLOTS + v, v, i + 1, SLOTS), False)
                        for g in range((turns + 1) * SLOTS, EG):
                            load_attr(Step(g, g % SLOTS, g // SLOTS, SLOTS), False)

                full = NG - 1 if n == 0 else NG
                to_full = NG - 1 if n == LAYERS - 1 else NG
                source = x_rows[n][0:full * GR, :].rearrange("(g t p) d -> g p t d", t=GROUP, p=P)
                target = x_rows[n + 1][0:to_full * GR, :].rearrange("(g t p) d -> g p t d", t=GROUP, p=P)

                store_lag = NORM_LAG[n] + 2

                def move(s, drain):
                    if not drain:
                        if past(s.g, SLOTS):
                            if n == 1:
                                sp.wait_ge(turn_done[1], s.g - (SLOTS - 1))
                                sp.wait_ge(pool_ready[1], s.g - (SLOTS - 1))
                            else:
                                sp.wait_ge((sums_done if n == 2 else sum_ready)[n], s.g - (SLOTS - 1))
                        if n == 0 and isinstance(s.g, int) and s.g == NG - 1:
                            r0 = (NG - 1) * GR
                            sp.dma_start(rows_in[:, s.slot, 0:LAST_FULL, :],
                                         x[r0:r0 + LAST_FULL * P, :].rearrange("(t p) d -> p t d", p=P)).then_inc(tail_loaded, 16)
                            sp.wait_ge(tail_loaded, 16)
                            sp.dma_start(rows_in[0:LAST_PART, s.slot, LAST_FULL, :], x[r0 + LAST_FULL * P:N, :])\
                                .then_inc(loaded[s.slot], 16)
                        else:
                            sp.dma_start(rows_in[:, s.slot, :, :], pick(source, s.g)).then_inc(loaded[s.slot], 16)
                    b = s.back(store_lag)
                    if not past(b.g, 0):
                        return
                    sp.wait_ge(normed[n], b.g + 1)
                    if n == LAYERS - 1 and isinstance(b.g, int) and b.g == NG - 1:
                        r0 = (NG - 1) * GR
                        sp.dma_start(out[r0:r0 + LAST_FULL * P, :].rearrange("(t p) d -> p t d", p=P),
                                     rows_sum[:, b.slot, 0:LAST_FULL, :]).then_inc(tail_stored, 16)
                        sp.dma_start(out[r0 + LAST_FULL * P:N, :], rows_sum[0:LAST_PART, b.slot, LAST_FULL, :])\
                            .then_inc(stored[b.slot], 16)
                    else:
                        sp.dma_start(pick(target, b.g), rows_sum[:, b.slot, :, :]).then_inc(stored[b.slot], 16)

                def all_moves():
                    head = 8
                    for g in range(head):
                        move(Step(g, g % SLOTS, g // SLOTS, SLOTS), False)
                    turns = (NG - 1 - head) // SLOTS
                    with sp.Fori(0, turns) as i:
                        for v in range(SLOTS):
                            at = head + v
                            move(Step(i * SLOTS + at, at % SLOTS, i + at // SLOTS, SLOTS), False)
                    for g in range(head + turns * SLOTS, NG + store_lag):
                        move(Step(g, g % SLOTS, g // SLOTS, SLOTS), g >= NG)

                def pair_moves(p, drain):
                    e = ahead(p, LEAD + 1)
                    if not drain and there(e):
                        load_attr(e, False)
                    for s in both(p):
                        if not drain or here(s.back(store_lag)):
                            move(s, drain)

                if n == 3:
                    side_by_side = sp.value_load(near[0:1, 0:1], min_val=0, max_val=1)
                    with sp.If(side_by_side > 0):
                        for g in range(LEAD + 1):
                            load_attr(Step(g, g, 0, SLOTS), False)
                        walk_pairs(sp, 4, 40, NG // 2, store_lag // 2 + 1, pair_moves)
                    with sp.Else():
                        all_attrs()
                        all_moves()
                else:
                    if n in EDGE:
                        all_attrs()
                    all_moves()
            sp.wait_ge(tail_stored, 16)
            all_stored(sp, LAYERS - 1)

        @block.gpsimd
        def _(pool):
            pool.memset(edge_rows_i[:, 1, :], 0)
            pool.memset(edge_rows_i[:, 3, :], -1).then_inc(pads_set, 1)
            pool.iota(part[:, :], pattern=[[0, 1]], base=0, channel_multiplier=1, allow_small_or_imprecise_dtypes=True)
            pool.iota(iota[:, :], pattern=[[1, P]], base=0, channel_multiplier=0, allow_small_or_imprecise_dtypes=True)
            pool.iota(iota16[:, :], pattern=[[1, P]], base=0, channel_multiplier=0, allow_small_or_imprecise_dtypes=True)
            pool.iota(tile16[:, :], pattern=[[1, NT]], base=0, channel_multiplier=0, allow_small_or_imprecise_dtypes=True)
            pool.iota(base[:, :], pattern=[[P, NT]], base=0, channel_multiplier=0, allow_small_or_imprecise_dtypes=True)
            pool.iota(edge_up[:, :], pattern=[[1, ET]], base=1, channel_multiplier=0, allow_small_or_imprecise_dtypes=True)
            pool.iota(edge_down[:, :], pattern=[[-1, ET]], base=ET, channel_multiplier=0, allow_small_or_imprecise_dtypes=True)
            pool.iota(clamp_f[:, :], pattern=[[1, 2 * ET]], base=0, channel_multiplier=0,
                      allow_small_or_imprecise_dtypes=True).then_inc(iotas_ready, 1)
            pool.iota(reach[0:1, :].rearrange("p (a b) -> p a b", b=2 * GROUP), pattern=[[GROUP, NT // (2 * GROUP)], [0, 2 * GROUP]],
                      base=GROUP * (LEAD - 1) - 1, channel_multiplier=0, allow_small_or_imprecise_dtypes=True)
            pool.memset(messages[:, ET, :], 0.0)
            pool.memset(attr6[:, :, :, :], 0.0)
            pool.memset(src_weight[:, ET:ET + 1], 0.0).then_inc(pads_set, 1)

            GATHER_LAG = GATHERS_IN_FLIGHT - 1

            def landed(n, j):
                turn = (n * ET + j) // GATHERS_IN_FLIGHT
                pool.wait_ge(gather_landed[(n * ET + j) % GATHERS_IN_FLIGHT], 16 * (turn + 1))
                pool.sem_inc(gathered, 1)

            def gather_group(n, e, tiles=range(GROUP)):
                if n in EDGE and tiles[0] == 0:
                    raw_free(pool, n, e)
                for t in tiles:
                    j = e * GROUP + t
                    pool.indirect_dma_start(
                        out=gathered_rows[n][:, e % SLOTS, t, :] if n in EDGE else messages[:, j, :], out_offset=None,
                        in_=x_rows[n][:, :], in_offset=bass.IndirectOffsetOnAxis(ap=src_index[:, j:j + 1], axis=0),
                    ).then_inc(gather_landed[(n * ET + j) % GATHERS_IN_FLIGHT], 16)
                    if j >= GATHER_LAG:
                        landed(n, j - GATHER_LAG)

            def gather_layer(n):
                for e in range(EG):
                    gather_group(n, e)
                for j in range(ET - GATHER_LAG, ET):
                    landed(n, j)

            pool.wait_ge(index_ready, 1)
            gather_layer(0)
            pool.wait_ge(first_ready, 1)
            pool.wait_ge(dst_rows_stored, 32)
            for k in range(2):
                for c in range(4):
                    pool.indirect_dma_start(
                        out=windows[0:QT, k, c, :], out_offset=None, in_=dst_rows_dram[:, :],
                        in_offset=bass.IndirectOffsetOnAxis(ap=first_i[0:QT, k, c:c + 1], axis=0),
                    ).then_inc(windows_gathered, 16)

            pool.wait_ge(gathered, ET)
            with pool.Fori(0, EG) as e:
                here_now = messages[:, bass.ds(e * GROUP, GROUP), :]
                pool.wait_ge(src_weight_ready, e + 1)
                pool.tensor_tensor(here_now, here_now, along(src_weight[:, bass.ds(e * GROUP, GROUP)], D), ALU.mult)\
                    .then_inc(own_scaled, 1)

            pool.wait_ge(roots_ready, 1)
            pool.wait_ge(tables_ready, 1)

            def second_hots(n, s, drain):
                p = s.back(1)
                if here(p):
                    pool.wait_ge(rel_copied[n], p.g + 1)
                if here(p) and past(p.g, HOTS):
                    pool.wait_ge(sums_done[n], p.g - (HOTS - 1))
                if not drain:
                    pool.tensor_copy(rel_here[:, s.slot, :], dst_rel[:, 1, bass.ds(s.g * GROUP, GROUP)])\
                        .then_inc(rel_copied[n], 1)
                if here(p):
                    for t in range(GROUP - HOTS_POOL[n], GROUP):
                        ins = pool.tensor_scalar(onehots[:, p.slot % HOTS, GROUP + t, :], iota[:, :],
                                                 rel_here[:, p.slot, t:t + 1], None, ALU.is_equal)
                    ins.then_inc(hots_pool[n], 1)

            def own_part(s, drain):
                second_hots(0, s, drain)
                if drain:
                    return
                rows_here(pool, 0, s)
                if past(s.g, SLOTS):
                    pool.wait_ge(mid_ready[0], s.g - (SLOTS - 1))
                pool.tensor_tensor(rows_pool[:, s.slot, :, :], rows_in[:, s.slot, :, :],
                                   along(dinv_sq[:, bass.ds(s.g * GROUP, GROUP)], D), ALU.mult).then_inc(pool_ready[0], 1)

            walk(pool, NG, SLOTS, 14, own_part, 1)

            all_stored(pool, 0)
            gather_layer(1)
            pool.wait_ge(biases_ready, 1)

            def biased_rows(s, drain):
                rows_here(pool, 1, s)
                if past(s.g, SLOTS):
                    pool.wait_ge(sum_ready[1], s.g - (SLOTS - 1))
                pool.tensor_tensor(rows_pool[:, s.slot, :, :], rows_in[:, s.slot, :, :],
                                   over(bias_all[:, B2B, :], GROUP), ALU.add).then_inc(pool_ready[1], 1)

            walk(pool, NG, SLOTS, 14, biased_rows, 0)
            all_stored(pool, 1)
            gather_layer(2)

            all_stored(pool, 2)
            side_by_side = pool.value_load(near[0:1, 0:1], min_val=0, max_val=1)
            with pool.If(side_by_side > 0):
                for e in range(EG + LEAD + 2):
                    if e == EG:
                        for j in range(ET - GATHER_LAG, ET):
                            landed(3, j)
                    for k in range(2):
                        if e < EG:
                            gather_group(3, e, (2 * k, 2 * k + 1))
                        g = (e - LEAD - 2) * 2 + k + 1
                        if g == 1:
                            second_hots(3, Step(0, 0, 0, SLOTS), False)
                        if g >= 1:
                            second_hots(3, Step(g, g % SLOTS, g // SLOTS, SLOTS), g >= NG)
            with pool.Else():
                gather_layer(3)
                walk(pool, NG, SLOTS, 14, lambda s, drain: second_hots(3, s, drain), 1)

        @block.tensor
        def _(pe):
            pe.wait_ge(idents_ready, 1)
            pe.wait_ge(rows_cast, 1)
            pe.transpose(bank[0][:, 0:P], edge_rows[:, 0, :], ident[:, :])
            pe.transpose(bank[0][:, P:ET], edge_rows[0:ROWS1, 1, :], ident[0:ROWS1, 0:ROWS1])
            pe.transpose(bank[1][:, 0:P], edge_rows[:, 2, :], ident[:, :])
            pe.transpose(bank[1][:, P:ET], edge_rows[0:ROWS1, 3, :], ident[0:ROWS1, 0:ROWS1]).then_inc(edges_turned, 1)

            def histogram(s, drain):
                first = isinstance(s.g, int) and s.g == 0
                last = drain
                pe.wait_ge(hot_ready, s.g + 1)
                pe.matmul(bank[2][:, 0:NT], place_hot[:, s.slot, :], tile_hot[:, s.slot, :], start=first, stop=False,
                          skip_group_check=True)
                for c in range(4):
                    mm = pe.matmul(bank[3 + c // 2][0:QT, bass.ds((c % 2) * ET + s.g, 1)],
                                   tile_hot[:, s.slot, c * QT:(c + 1) * QT], ones16[:, 0:1], start=True, stop=True,
                                   skip_group_check=True)
                mm.then_inc(hist_done, 1)

            walk(pe, ET, RING, RING, histogram, 0, 4)

            pe.wait_ge(weights_loaded, 16 * len(mats))
            pe.transpose(bank[6][:, 0:P], w1b_s, ident[:, :]).then_inc(fold_turned, 1)
            pe.matmul(bank[5][:, :], ones[0:1, :], bias_row.rearrange("a n d -> a (n d)"), start=True, stop=True)
            pe.wait_ge(fold_copied, 1)
            pe.matmul(bank[6][:, 0:D], w1b_t, w2am_s, start=True, stop=True)
            pe.matmul(bank[6][:, D:2 * D], b1b_wide, w2am_s, start=True, stop=True)
            pe.matmul(bank[6][:, 2 * D:2 * D + 1], w2au_s, u_col, start=True, stop=True).then_inc(folded, 1)

            pe.wait_ge(span_ready, 1)
            for c in range(4):
                pe.transpose(bank[0][0:1, c * QT:(c + 1) * QT], first_f[0:QT, 0, c:c + 1], ident[0:QT, 0:QT])
            pe.transpose(bank[1][0:1, 0:QT], widest[0:QT, :], ident[0:QT, 0:QT]).then_inc(span_turned, 1)

            pe.wait_ge(count16_ready, 1)
            pe.wait_ge(folds_copied, 1)

            def pick_rows(s, drain, parts):
                if not drain:
                    if s.slot < ACT_HOTS:
                        pe.wait_ge(src_hot_ready, s.turn * ACT_HOTS + (s.slot + 1))
                    else:
                        pe.wait_ge(src_hot_dve, s.turn + 1)
                    if past(s.g, 2):
                        pe.wait_ge(src_hot_copied, s.g - 1)
                    pe.transpose(turned16[s.slot % 2], place_hot[:, s.slot, :], ident16).then_inc(src_hot_turned, 1)
                b = s.back(2)
                if not inside(b):
                    return
                pe.wait_ge(src_hot_copied, b.g + 1)
                if past(b.g, 2):
                    pe.wait_ge(src_picked, b.g - 1)
                for n, part in enumerate(parts):
                    mm = pe.matmul(bank[2 + b.slot % 2][:, 0:NT], place_hot_t[:, b.slot, :], count16[:, part, :],
                                   start=(n == 0), stop=(n == len(parts) - 1))
                mm.then_inc(src_counted, 1)

            pe.wait_ge(first_ready, 1)
            wide = pe.value_load(width[0:1, 0:1], min_val=0, max_val=ET - 2)
            with pe.If(wide > 0):
                walk(pe, ET, RING, RING, lambda s, drain: pick_rows(s, drain, (0, 1)), 2, 4)
            with pe.Else():
                walk(pe, ET, RING, RING, lambda s, drain: pick_rows(s, drain, (2,)), 2, 4)

            pe.wait_ge(windows_gathered, 16 * 8)
            pe.wait_ge(near_ready, 1)
            for k in range(2):
                for c in range(4):
                    mm = pe.transpose(bank[k][:, c * QT:(c + 1) * QT], windows[0:QT, k, c, :], ident[0:QT, 0:QT])
            mm.then_inc(windows_turned, 1)
            pe.wait_ge(tables_ready, 1)
            others = pe.value_load(width[0:1, 0:1], min_val=0, max_val=ET - 2)

            def sum_messages(n, s, only_first=False):
                to = summed[s.slot % SUM_BANKS[n]]
                firsts = nc.values_load_multi_w_load_instructions(
                    first_row[0:1, bass.ds(s.g * GROUP, GROUP)], engines=[mybir.EngineType.PE], min_val=0, max_val=ET - 2,
                    skip_runtime_bounds_check_because="the first tiles are held at most ET - 2 where they are made")[1]
                pe.wait_ge(hots_ready[n], s.g + 1)
                if n in hots_pool:
                    pe.wait_ge(hots_pool[n], s.g + 1)
                for t in range(GROUP):
                    for k in range(2):
                        mm = pe.matmul(to[:, t, :], onehots[:, s.slot % HOTS, k * GROUP + t, :],
                                       messages[:, bass.ds(firsts[t] + k, 1), :].rearrange("p a d -> p (a d)"),
                                       start=(t == 0 and k == 0), stop=(n != 2 and t == GROUP - 1 and k == 1),
                                       skip_group_check=True)
                if n == 2:
                    rows_here(pe, 2, s)
                    mm = pe.matmul(to, ident[:, :], rows_in[:, s.slot, :, :], start=False, stop=True, skip_group_check=True)
                mm.then_inc(sums_done[n], 1)
                if only_first:
                    return
                with pe.If(others > 0):
                    pe.wait_ge(gathered, (n + 1) * ET)
                    for t in range(GROUP):
                        with pe.Fori(0, others) as k:
                            j = pe.value_load(clamp[0:1, bass.ds(firsts[t] + (k + 2), 1)], min_val=0, max_val=ET)
                            pe.wait_ge(extra_ready[n], (s.g * GROUP + t) * others + (k + 1))
                            pe.matmul(to[:, t, :], extra_hot[:, :],
                                      messages[:, bass.ds(j, 1), :].rearrange("p a d -> p (a d)"),
                                      start=False, stop=False, skip_group_check=True).then_inc(extra_used[n], 1)

            def turn_rows(to, rows, done):
                for t in range(GROUP):
                    mm = pe.transpose(to[:, t * P:(t + 1) * P], rows[:, t, :], ident[:, :])
                mm.then_inc(done, 1)

            pe.wait_ge(own_scaled, EG)
            pe.wait_ge(biases_ready, 1)
            pe.sem_inc(extra_used[0], 1)

            def layer0(s, drain):
                if not drain:
                    if past(s.g, 2):
                        pe.wait_ge(scaled_ready[0], s.g - 1)
                    sum_messages(0, s)
                q = s.back(3)
                if here(q):
                    pe.wait_ge(turn_copied[0], q.g + 1)
                    if past(q.g, 2):
                        pe.wait_ge(sum_ready[0], q.g - 1)
                    to = product[q.slot % 2]
                    for t in range(GROUP):
                        pe.matmul(tiled(to)[:, t, :], turned[:, q.slot % 2, t * P:(t + 1) * P], w0_s[:, :],
                                  start=(t == 0), stop=False, skip_group_check=True)
                    pe.matmul(to[:, :], ones_b[:, :], bias0_parts[:, :, :].rearrange("p t d -> p (t d)"),
                              start=False, stop=True, skip_group_check=True).then_inc(product_done[0], 1)
                p = s.back(2)
                if here(p):
                    pe.wait_ge(mid_ready[0], p.g + 1)
                    if past(p.g, 2):
                        pe.wait_ge(turn_copied[0], p.g - 1)
                    turn_rows(turning[p.slot % 2], rows_mid[:, p.slot % 2, :, :], turn_done[0])

            walk(pe, NG, SLOTS, 14, layer0, 3)

            def turn_edges(n, e):
                pe.wait_ge(gathered, e.g * GROUP + (n * ET + GROUP))
                pe.wait_ge(attr_loaded[e.slot], 16 * (EDGE.index(n) * len(range(e.slot, EG, SLOTS)) + e.turn + 1))
                for_x, for_attr = (bank[2], bank[3]) if n == 1 else (bank[6], bank[7])
                if past(e.g, 1):
                    pe.wait_ge(e_copied_x[n], e.g)
                    pe.wait_ge(e_copied_a[n], e.g)
                for t in range(GROUP):
                    pe.transpose(for_x[:, t * P:(t + 1) * P], gathered_rows[n][:, e.slot, t, :], ident[:, :])
                for t in range(GROUP):
                    if n == 1:
                        mm = pe.transpose(for_attr[:, t * P:(t + 1) * P], attr[:, e.slot, t, :], ident[:, :])
                    else:
                        mm = pe.transpose(for_attr[0:EF, t * P:(t + 1) * P], attr6[:, e.slot, t, :], ident[:, :])
                mm.then_inc(e_turned[n], 1)

            def edges1(e, drain):
                if not drain:
                    turn_edges(1, e)
                p = e.back(1)
                if past(p.g, 0):
                    b = p.slot % 2
                    pe.wait_ge(e_relu, p.g + 1)
                    if past(p.g, 2):
                        pe.wait_ge(messages_ready[1], p.g - 1)
                    for t in range(GROUP):
                        mm = pe.matmul(tiled(product[b])[:, t, :], turned2[:, b, t * P:(t + 1) * P], w1m[:, :],
                                       start=(t == 0), stop=(t == GROUP - 1), skip_group_check=True)
                    mm.then_inc(e_product[1], 1)
                if not drain:
                    b = e.slot % 2
                    pe.wait_ge(e_copied_x[1], e.g + 1)
                    pe.wait_ge(e_copied_a[1], e.g + 1)
                    if past(e.g, 2):
                        pe.wait_ge(e_relu, e.g - 1)
                    pe.matmul(bank[b][:, :], w1a_s[:, 0, :], turned[:, b, :], start=True, stop=False)
                    pe.matmul(bank[b][:, :], w1a_s[:, 1, :], attr_turned[:, b, :], start=False, stop=True).then_inc(e_hidden, 1)

            walk(pe, EG, SLOTS, 7, edges1, 1, 1)

            pe.wait_ge(messages_ready[1], EG)
            pe.sem_inc(extra_used[1], 1)

            def layer1(s, drain):
                b = s.slot % 2
                if not drain:
                    rows_here(pe, 1, s)
                    if past(s.g, 4):
                        pe.wait_ge(hidden_copied, s.g - 3)
                    turn_rows(turning[b], rows_in[:, s.slot, :, :], turn_done[1])
                    if past(s.g, 2):
                        pe.wait_ge(scaled_ready[1], s.g - 1)
                    sum_messages(1, s)
                    pe.wait_ge(turn_copied[1], s.g + 1)
                    if past(s.g, 2):
                        pe.wait_ge(mid_ready[1], s.g - 1)
                    for t in range(GROUP):
                        mm = pe.matmul(tiled(product[b])[:, t, :], turned[:, b, t * P:(t + 1) * P], w2ax_s[:, :],
                                       start=(t == 0), stop=(t == GROUP - 1), skip_group_check=True)
                    mm.then_inc(product_done[1], 1)
                p = s.back(2)
                if here(p):
                    pe.wait_ge(mid_ready[1], p.g + 1)
                    turn_rows(turning[b], rows_mid[:, b, :, :], hidden_turned)
                q = s.back(3)
                if here(q):
                    pe.wait_ge(hidden_copied, q.g + 1)
                    if past(q.g, 2):
                        pe.wait_ge(sum_ready[1], q.g - 1)
                    for t in range(GROUP):
                        mm = pe.matmul(tiled(update[q.slot % 2])[:, t, :], turned2[:, q.slot % 2, t * P:(t + 1) * P],
                                       w2b_s[:, :], start=(t == 0), stop=(t == GROUP - 1), skip_group_check=True)
                    mm.then_inc(update_done, 1)

            walk(pe, NG, SLOTS, 14, layer1, 3)

            pe.sem_inc(extra_used[2], 1)

            def layer2(s, drain, only_first=False):
                if past(s.g, SLOTS):
                    pe.wait_ge(normed[2], s.g - (SLOTS - 1))
                sum_messages(2, s, only_first)

            def pairs2(p, drain):
                ready = p.g + (LEAD - 1)
                pe.wait_ge(learned_scaled, min(ready, EG) if isinstance(ready, int) else ready)
                for s in both(p):
                    layer2(s, False, True)

            side_by_side = pe.value_load(near[0:1, 0:1], min_val=0, max_val=1)
            with pe.If(side_by_side > 0):
                walk_pairs(pe, 9, EG - LEAD, NG // 2, 0, pairs2)
            with pe.Else():
                pe.wait_ge(learned_scaled, EG)
                walk(pe, NG, SLOTS, 14, layer2, 0)
            pe.sem_inc(extra_used[3], 1)

            def edges3(e, drain):
                if not drain:
                    turn_edges(3, e)
                p = e.back(1)
                if not past(p.g, 0):
                    return
                b = p.slot % 2
                pe.wait_ge(e_copied_x[3], p.g + 1)
                pe.wait_ge(e_copied_a[3], p.g + 1)
                if past(p.g, 2):
                    pe.wait_ge(messages_ready[3], p.g - 1)
                for t in range(GROUP):
                    pe.matmul(tiled(product[b])[:, t, :], turned[:, b, t * P:(t + 1) * P], w3_s[:, :],
                              start=(t == 0), stop=False, skip_group_check=True)
                    mm = pe.matmul(tiled(product[b])[:, t, :], attr_turned[0:EF, b, t * P:(t + 1) * P], we_s[:, :],
                                   start=False, stop=(t == GROUP - 1), skip_group_check=True)
                mm.then_inc(e_product[3], 1)

            def layer3(s, drain, only_first=False):
                if past(s.g, 3):
                    pe.wait_ge(sum_ready[3], s.g - 2)
                sum_messages(3, s, only_first)

            def pairs3(p, drain):
                e = ahead(p, LEAD)
                if there(e) or e.g == EG:
                    edges3(e, not there(e))
                ready = p.g + (LEAD - 1)
                pe.wait_ge(messages_ready[3], min(ready, EG) if isinstance(ready, int) else ready)
                for s in both(p):
                    layer3(s, False, True)

            with pe.If(side_by_side > 0):
                for g in range(LEAD):
                    edges3(Step(g, g, 0, SLOTS), False)
                walk_pairs(pe, 9, EG - LEAD, NG // 2, 0, pairs3)
            with pe.Else():
                walk(pe, EG, SLOTS, 7, edges3, 1, 1)
                pe.wait_ge(messages_ready[3], EG)
                walk(pe, NG, SLOTS, 14, layer3, 0)

        @block.scalar
        def _(act):
            act.wait_ge(count_ready, 1)
            act.activation(dinv[:, :], count, ACT.Sqrt, bias=1.0).then_inc(count_root, 1)

            act.wait_ge(fold_turned, 1)
            act.copy(w1b_t, bank[6][:, 0:P])
            act.copy(b1b_wide, bias_cols[:, 1:2].to_broadcast([P, P])).then_inc(fold_copied, 1)
            act.wait_ge(folded, 1)
            act.copy(w1m[:, :], bank[6][:, 0:D])
            act.copy(b1m_all[:, :], bank[6][:, D:2 * D])
            act.activation(bias_cols[:, 3:4], bank[6][:, 2 * D:2 * D + 1], ACT.Identity, bias=bias_cols[:, 2:3])
            act.copy(bias_all[:, :, :], tiled(bank[5])).then_inc(folds_copied, 1)

            def hot_src(s, drain):
                if inside(s) and s.slot < ACT_HOTS:
                    if past(s.turn, 1):
                        act.wait_ge(src_hot_ready, s.turn * ACT_HOTS + (s.slot + 1 - ACT_HOTS))
                    act.activation(distance[:, s.slot, :], iota16, ACT.Abs, scale=-1.0,
                                   bias=split[:, SRC_PLACE, bass.ds(s.g, 1)]).then_inc(src_distance, 1)
                h = s.back(1)
                if inside(h) and h.slot < ACT_HOTS:
                    act.wait_ge(src_distance, h.turn * ACT_HOTS + (h.slot + 1))
                    if past(h.g, RING):
                        act.wait_ge(src_hot_turned, h.g - (RING - 1))
                    act.activation(place_hot[:, h.slot, :], distance[:, h.slot, :], ACT.Relu, scale=-1.0, bias=1.0)\
                        .then_inc(src_hot_ready, 1)
                c = s.back(2)
                if inside(c):
                    act.wait_ge(src_hot_turned, c.g + 1)
                    if past(c.g, RING):
                        act.wait_ge(src_counted, c.g - (RING - 1))
                    act.copy(place_hot_t[:, c.slot, :], turned16[c.slot % 2]).then_inc(src_hot_copied, 1)
                r = s.back(8)
                if inside(r) and r.slot == RING - 1:
                    act.wait_ge(src_picked, r.g + 1)
                    act.activation(src_weight[:, bass.ds(r.turn * GROUP, GROUP)], src_count[:, bass.ds(r.turn * GROUP, GROUP)],
                                   ACT.Sqrt, bias=1.0).then_inc(src_root, 1)

            walk(act, ET, RING, 5 * RING, hot_src, 8, 4)

            act.wait_ge(tables_ready, 1)
            act_others = act.value_load(width[0:1, 0:1], min_val=0, max_val=ET - 2)

            def norm(n, z):
                act.wait_ge(scale_done[n], z.g + 1)
                if n == 2 and past(z.turn, 1):
                    rows_out(act, n, z.slot, z.turn)
                whole = summed[z.slot] if n == 2 else rows_sum[:, z.slot, :, :]
                for t in range(GROUP):
                    ins = act.activation(rows_sum[:, z.slot, t, :], whole[:, t, :], ACT.Identity,
                                         scale=scale[:, z.slot, t, 1:2], bias=scale[:, z.slot, t, 2:3])
                ins.then_inc(normed[n], 1)

            def std(n, r):
                act.wait_ge(moments_done[n], r.g + 1)
                act.activation(scale[:, r.slot, :, 0], moments[:, r.slot, :, 1], ACT.Sqrt, bias=eps[:, :])\
                    .then_inc(std_done[n], 1)

            def scaled_sums(n, p, by):
                b = p.slot % 2
                act.wait_ge(sums_done[n], p.g + 1)
                act.wait_ge(extra_used[n], (p.g * GROUP + GROUP) * act_others + 1)
                if past(p.g, 2):
                    act.wait_ge(mid_ready[n], p.g - 1)
                for t in range(GROUP):
                    ins = act.activation(rows_scaled[:, b, t, :], summed[b][:, t, :], ACT.Copy,
                                         scale=by[:, bass.ds(p.g * GROUP + t, 1)])
                ins.then_inc(scaled_ready[n], 1)

            def act0(s, drain):
                c, p, z, r = s.back(3), s.back(1), s.back(5), s.back(4)
                if here(c):
                    act.wait_ge(turn_done[0], c.g + 1)
                    if past(c.g, 2):
                        act.wait_ge(product_done[0], c.g - 1)
                    act.copy(turned[:, c.slot % 2, :], turning[c.slot % 2][:, :]).then_inc(turn_copied[0], 1)
                if here(p):
                    scaled_sums(0, p, dinv)
                if here(r):
                    std(0, r)
                if here(z):
                    norm(0, z)

            walk(act, NG, SLOTS, 14, act0, 5)

            def act_edges1(e, drain):
                b = e.slot % 2
                act.wait_ge(e_turned[1], e.g + 1)
                if past(e.g, 2):
                    act.wait_ge(e_hidden, e.g - 1)
                act.copy(turned[:, b, :], bank[2][:, :]).then_inc(e_copied_x[1], 1)
                act.wait_ge(e_hidden, e.g + 1)
                if past(e.g, 2):
                    act.wait_ge(e_product[1], e.g - 1)
                act.activation(turned2[:, b, :], bank[b][:, :], ACT.Relu, bias=bias_cols[:, 0:1]).then_inc(e_relu, 1)

            walk(act, EG, SLOTS, 7, act_edges1, 0, 1)

            def act1(s, drain):
                b = s.slot % 2
                if not drain:
                    act.wait_ge(turn_done[1], s.g + 1)
                    if past(s.g, 2):
                        act.wait_ge(product_done[1], s.g - 1)
                    act.copy(turned[:, b, :], turning[b][:, :]).then_inc(turn_copied[1], 1)
                c, z, r = s.back(3), s.back(5), s.back(4)
                if here(c):
                    act.wait_ge(hidden_turned, c.g + 1)
                    if past(c.g, 2):
                        act.wait_ge(update_done, c.g - 1)
                    act.activation(turned2[:, c.slot % 2, :], turning[c.slot % 2][:, :], ACT.Relu,
                                   bias=bias_cols[:, 3:4]).then_inc(hidden_copied, 1)
                if here(r):
                    std(1, r)
                if here(z):
                    norm(1, z)
                if not drain:
                    scaled_sums(1, s, rcount)

            walk(act, NG, SLOTS, 14, act1, 5)

            def act_nodes(n, s, drain):
                z, r = s.back(NORM_LAG[n]), s.back(NORM_LAG[n] - 1)
                if here(r):
                    std(n, r)
                if here(z):
                    norm(n, z)

            def scale_messages(e):
                group = messages[:, bass.ds(e.g * GROUP, GROUP), :]
                act.wait_ge(gathered, e.g * GROUP + (2 * ET + GROUP))
                act.activation(group, group, ACT.Copy, scale=learned_all[:, :]).then_inc(learned_scaled, 1)

            def act_pairs2(p, drain):
                e = ahead(p, LEAD)
                first, second = both(p)
                act_nodes(2, first, drain)
                if there(e):
                    scale_messages(e)
                act_nodes(2, second, drain)

            side_by_side = act.value_load(near[0:1, 0:1], min_val=0, max_val=1)
            with act.If(side_by_side > 0):
                for g in range(LEAD):
                    scale_messages(Step(g, g, 0, SLOTS))
                walk_pairs(act, 9, EG - LEAD, NG // 2, 2, act_pairs2)
            with act.Else():
                walk(act, EG, SLOTS, 7, lambda e, drain: scale_messages(e), 0, 1)
                walk(act, NG, SLOTS, 14, lambda s, drain: act_nodes(2, s, drain), NORM_LAG[2])

            def act_edges3(e, drain):
                b = e.slot % 2
                act.wait_ge(e_turned[3], e.g + 1)
                if past(e.g, 2):
                    act.wait_ge(e_product[3], e.g - 1)
                act.copy(turned[:, b, :], bank[6][:, :]).then_inc(e_copied_x[3], 1)

            def act_pairs(p, drain):
                e = ahead(p, LEAD)
                first, second = both(p)
                act_nodes(3, first, drain)
                if there(e):
                    act_edges3(e, False)
                act_nodes(3, second, drain)

            with act.If(side_by_side > 0):
                for g in range(LEAD):
                    act_edges3(Step(g, g, 0, SLOTS), False)
                walk_pairs(act, 9, EG - LEAD, NG // 2, 2, act_pairs)
            with act.Else():
                walk(act, EG, SLOTS, 7, act_edges3, 0, 1)
                walk(act, NG, SLOTS, 14, lambda s, drain: act_nodes(3, s, drain), NORM_LAG[3])

        @block.vector
        def _(dve):
            steps = [0]

            def then(ins):
                steps[0] += 1
                ins.then_inc(prologue_step, 1)
                dve.wait_ge(prologue_step, steps[0])

            dve.wait_ge(iotas_ready, 1)
            dve.tensor_scalar(ident[:, :], iota[:, :], part, None, ALU.is_equal)
            dve.tensor_scalar(ident16, iota16, part, None, ALU.is_equal)
            dve.memset(ones, 1.0)
            dve.memset(ones16, 1.0)
            dve.memset(eps[:, :], EPS)
            dve.memset(dst_cols[:, ET:ET + 1], -1.0)
            dve.tensor_scalar(clamp[0:1, :], clamp_f[0:1, :], float(ET), None, ALU.min).then_inc(idents_ready, 1)
            dve.wait_ge(edges_loaded, 16 * 6)
            dve.tensor_copy(edge_rows, edge_rows_i).then_inc(rows_cast, 1)
            dve.wait_ge(edges_turned, 1)
            dve.tensor_copy(src_index[:, :], bank[0][:, 0:ET]).then_inc(index_ready, 1)
            dve.tensor_copy(dst_cols[:, 0:ET], bank[1][:, 0:ET])
            then(dve.tensor_copy(dst_index, bank[1][:, 0:ET]))
            dve.wait_ge(index_ready, 1)
            for n, ids in ((SRC_TILE, src_index[:, :]), (DST_TILE, dst_index)):
                dve.tensor_scalar(split_i[:, n, :], ids, 7, None, ALU.arith_shift_right)
                ins = dve.tensor_scalar(split_i[:, n + 1, :], ids, P - 1, None, ALU.bitwise_and)
            then(ins)
            then(dve.tensor_copy(split, split_i))

            def hots_dst(s, drain):
                if past(s.g, RING):
                    dve.wait_ge(hist_done, s.g - (RING - 1))
                dve.tensor_scalar(place_hot[:, s.slot, :], iota16, split[:, DST_PLACE, bass.ds(s.g, 1)], None, ALU.is_equal)
                dve.tensor_scalar(tile_hot[:, s.slot, :], tile16, split[:, DST_TILE, bass.ds(s.g, 1)], None, ALU.is_equal)\
                    .then_inc(hot_ready, 1)

            walk(dve, ET, RING, RING, hots_dst, 0, 4)
            dve.wait_ge(hist_done, ET)
            dve.tensor_copy(count, bank[2][:, 0:NT]).then_inc(count_ready, 1)
            then(dve.tensor_copy(count_i, bank[2][:, 0:NT]))
            dve.wait_ge(count_ready, 1)
            then(dve.tensor_scalar(count_i, count_i, 255, None, ALU.bitwise_and))
            dve.tensor_copy(count16[:, 1, :], count_i)
            then(dve.tensor_copy(count_low_f, count_i))
            dve.tensor_copy(count16[:, 2, :], count)
            dve.tensor_tensor(count16[:, 0, :], count, count_low_f, ALU.subtract).then_inc(count16_ready, 1)
            for n, ramp in ((0, edge_up), (1, edge_down)):
                for c in range(4):
                    ins = dve.scalar_tensor_tensor(present[0:QT, c, :], bank[3 + c // 2][0:QT, (c % 2) * ET:(c % 2 + 1) * ET],
                                                   0.0, ramp[0:QT, :], ALU.is_gt, ALU.mult)
                then(ins)
                then(dve.tensor_reduce(span[0:QT, n, :], present[0:QT, :, :], AX_X, ALU.max))
            then(dve.tensor_scalar(first_f[0:QT, 1, :], span[0:QT, 1, :], -1.0, float(ET), ALU.mult, ALU.add))
            then(dve.tensor_scalar(first_f[0:QT, 0, :], first_f[0:QT, 1, :], float(ET - 2), None, ALU.min))
            dve.tensor_copy(first_i[0:QT, 0, :], first_f[0:QT, 0, :])
            dve.tensor_scalar(first_i[0:QT, 1, :], first_f[0:QT, 0, :], 1.0, None, ALU.add)
            then(dve.tensor_tensor(first_f[0:QT, 2, :], span[0:QT, 0, :], first_f[0:QT, 0, :], ALU.subtract))
            dve.tensor_reduce(widest[0:QT, :], first_f[0:QT, 2, :], AX_X, ALU.max).then_inc(span_ready, 1)
            dve.wait_ge(span_turned, 1)
            dve.tensor_copy(first_row[0:1, :], bank[0][0:1, 0:NT])
            then(dve.tensor_reduce(width_f[0:1, :], bank[1][0:1, 0:QT], AX_X, ALU.max))
            dve.tensor_scalar(width[0:1, :], width_f[0:1, :], 2.0, -2.0, ALU.max, ALU.add).then_inc(first_ready, 1)
            dve.wait_ge(pads_set, 2)
            then(dve.tensor_tensor(reach[0:1, :], bank[0][0:1, 0:NT], reach[0:1, :], ALU.subtract))
            then(dve.tensor_reduce(span[0:1, 0, 0:1], reach[0:1, :], AX_X, ALU.max))
            dve.tensor_scalar(span[0:1, 0, 1:2], span[0:1, 0, 0:1], -1.0, None, ALU.is_le)
            then(dve.tensor_scalar(span[0:1, 0, 2:3], width_f[0:1, :], 2.0, None, ALU.is_le))
            dve.tensor_tensor(near[0:1, :], span[0:1, 0, 1:2], span[0:1, 0, 2:3], ALU.mult).then_inc(near_ready, 1)
            then(dve.tensor_scalar(rcount[:, :], count, 1.0, None, ALU.max))
            dve.reciprocal(rcount[:, :], rcount[:, :])
            dve.wait_ge(count_root, 1)
            then(dve.reciprocal(dinv[:, :], dinv[:, :]))
            dve.tensor_tensor(dinv_sq[:, :], dinv[:, :], dinv[:, :], ALU.mult).then_inc(roots_ready, 1)

            def count_src(s, drain):
                if inside(s) and s.slot >= ACT_HOTS:
                    if past(s.g, RING):
                        dve.wait_ge(src_hot_turned, s.g - (RING - 1))
                    dve.tensor_scalar(place_hot[:, s.slot, :], iota16, split[:, SRC_PLACE, bass.ds(s.g, 1)], None,
                                      ALU.is_equal).then_inc(src_hot_dve, 1)
                b = s.back(3)
                if inside(b):
                    dve.wait_ge(src_counted, b.g + 1)
                    if past(b.g, 2):
                        dve.wait_ge(src_picked, b.g - 1)
                    dve.scalar_tensor_tensor(picked[:, b.slot % 2, :], tile16, split[:, SRC_TILE, bass.ds(b.g, 1)],
                                             bank[2 + b.slot % 2][:, 0:NT], ALU.is_equal, ALU.mult,
                                             accum_out=src_count[:, bass.ds(b.g, 1)]).then_inc(src_picked, 1)
                r = s.back(12)
                if inside(r) and r.slot == RING - 1:
                    dve.wait_ge(src_root, r.turn + 1)
                    rooted = src_weight[:, bass.ds(r.turn * GROUP, GROUP)]
                    dve.reciprocal(rooted, rooted).then_inc(src_weight_ready, 1)

            walk(dve, ET, RING, 5 * RING, count_src, 12, 4)
            dve.wait_ge(folds_copied, 1)
            dve.tensor_tensor(bias_all[:, B3E, :], bias_all[:, B3E, :], bias_all[:, 3, :], ALU.add)
            whole, left, pick = parts_f[:, 0, :], parts_f[:, 1, :], parts_f[:, 2, :]
            then(dve.tensor_copy(whole, bias_all[:, BIAS0, :]))
            for n in range(3):
                then(dve.tensor_copy(part_b, whole))
                then(dve.tensor_tensor(left, whole, part_b, ALU.subtract))
                then(dve.tensor_scalar(on_part, part, float(n), None, ALU.is_equal))
                if n == 0:
                    then(dve.tensor_scalar(pick, part_b, on_part, None, ALU.mult))
                else:
                    then(dve.scalar_tensor_tensor(pick, part_b, on_part, pick, ALU.mult, ALU.add))
                then(dve.tensor_copy(whole, left))
            dve.memset(ones_b[:, :], 1.0)
            dve.tensor_copy(bias0_parts[:, :, :], over(pick, GROUP)).then_inc(biases_ready, 1)

            dve.wait_ge(windows_turned, 1)
            for k in range(2):
                ins = dve.tensor_tensor(dst_rel[:, k, :], bank[k][:, 0:NT], base[:, :], ALU.subtract)
            ins.then_inc(tables_ready, 1)
            dve.wait_ge(tables_ready, 1)
            others = dve.value_load(width[0:1, 0:1], min_val=0, max_val=ET - 2)

            def hots(n, s):
                if past(s.g, HOTS):
                    dve.wait_ge(sums_done[n], s.g - (HOTS - 1))
                hots_of(dve, s, 2 * GROUP - HOTS_POOL.get(n, 0)).then_inc(hots_ready[n], 1)

            def extras(n, p):
                with dve.If(others > 0):
                    for t in range(GROUP):
                        first = dve.value_load(first_row[0:1, bass.ds(p.g * GROUP + t, 1)], min_val=0, max_val=ET - 2)
                        with dve.Fori(0, others) as k:
                            j = dve.value_load(clamp[0:1, bass.ds(first + (k + 2), 1)], min_val=0, max_val=ET)
                            so_far = (p.g * GROUP + t) * others + (k + 1)
                            dve.wait_ge(extra_used[n], so_far)
                            dve.tensor_tensor(extra_rel[:, :], dst_cols[:, bass.ds(j, 1)],
                                              base[:, bass.ds(p.g * GROUP + t, 1)], ALU.subtract).then_inc(extra_step[n], 1)
                            dve.wait_ge(extra_step[n], so_far)
                            dve.tensor_scalar(extra_hot[:, :], iota[:, :], extra_rel[:, :], None, ALU.is_equal)\
                                .then_inc(extra_ready[n], 1)
                dve.wait_ge(extra_used[n], (p.g * GROUP + GROUP) * others + 1)

            def inverse(n, z):
                dve.wait_ge(std_done[n], z.g + 1)
                dve.reciprocal(scale[:, z.slot, :, 1], scale[:, z.slot, :, 0]).then_inc(inv_done[n], 1)

            def shift(n, z):
                dve.wait_ge(inv_done[n], z.g + 1)
                dve.scalar_tensor_tensor(scale[:, z.slot, :, 2], moments[:, z.slot, :, 0], -1.0, scale[:, z.slot, :, 1],
                                         ALU.mult, ALU.mult).then_inc(scale_done[n], 1)

            def statistics(n, r):
                b = r.slot % 2
                dve.wait_ge((sums_done if n == 2 else sum_ready)[n], r.g + 1)
                whole = summed[r.slot] if n == 2 else rows_sum[:, r.slot, :, :]
                for t in range(GROUP):
                    ins = dve.bn_stats(stats[:, b, t, :], whole[:, t, :])
                ins.then_inc(stats_done[n], 1)

            def aggregate(n, r):
                b = r.slot % 2
                for t in range(GROUP):
                    ins = dve.bn_aggr(moments[:, r.slot, t, :], stats[:, b, t, :])
                ins.then_inc(moments_done[n], 1)

            def sum_free(n, r):
                if past(r.turn, 1):
                    rows_out(dve, n, r.slot, r.turn)

            def layer_step(n, middle, total, middle_lag, by_pairs=False):
                sum_lag = NORM_LAG[n] - 1

                def step(s, drain):
                    if not drain:
                        hots(n, s)
                    e = s.back(min(1, sum_lag))
                    if here(e) and not by_pairs:
                        extras(n, e)
                    p, r, z = s.back(middle_lag), s.back(sum_lag), s.back(sum_lag + 1)
                    if middle is not None and here(p):
                        middle(p)
                    if here(z):
                        inverse(n, z)
                    if here(r):
                        if total is not None:
                            sum_free(n, r)
                            total(r).then_inc(sum_ready[n], 1)
                        statistics(n, r)
                        dve.wait_ge(stats_done[n], r.g + 1)
                    if here(z):
                        shift(n, z)
                    if here(r):
                        aggregate(n, r)

                if not by_pairs:
                    walk(dve, NG, SLOTS, 14, step, sum_lag + 1)
                    return

                def pairs(p, drain):
                    e = ahead(p, LEAD)
                    first, second = both(p)
                    step(first, drain)
                    if there(e) or e.g == EG:
                        dve_edges(n, e, not there(e))
                    step(second, drain)

                for g in range(LEAD):
                    dve_edges(n, Step(g, g, 0, SLOTS), False)
                walk_pairs(dve, 9, EG - LEAD, NG // 2, (sum_lag + 1) // 2 + 1, pairs)

            def middle0(p):
                b = p.slot % 2
                dve.wait_ge(scaled_ready[0], p.g + 1)
                dve.wait_ge(pool_ready[0], p.g + 1)
                if past(p.g, 2):
                    dve.wait_ge(turn_done[0], p.g - 1)
                dve.tensor_tensor(rows_mid[:, b, :, :], rows_scaled[:, b, :, :], rows_pool[:, p.slot, :, :], ALU.add)\
                    .then_inc(mid_ready[0], 1)

            def total0(r):
                dve.wait_ge(product_done[0], r.g + 1)
                return dve.scalar_tensor_tensor(rows_sum[:, r.slot, :, :], tiled(product[r.slot % 2]), 0.0,
                                                rows_in[:, r.slot, :, :], ALU.max, ALU.add)

            layer_step(0, middle0, total0, 2)

            def dve_edges(n, e, drain):
                b = e.slot % 2
                if not drain:
                    used = e_hidden if n == 1 else e_product[3]
                    dve.wait_ge(e_turned[n], e.g + 1)
                    if past(e.g, 2):
                        dve.wait_ge(used, e.g - 1)
                    rows = P if n == 1 else EF
                    dve.tensor_copy(attr_turned[0:rows, b, :], bank[3 if n == 1 else 7][0:rows, :]).then_inc(e_copied_a[n], 1)
                p = e.back(1)
                if past(p.g, 0):
                    dve.wait_ge(e_product[n], p.g + 1)
                    bias = b1m_all[:, :] if n == 1 else bias_all[:, B3E, :]
                    dve.tensor_tensor(messages[:, bass.ds(p.g * GROUP, GROUP), :], tiled(product[p.slot % 2]), over(bias, GROUP),
                                      ALU.add).then_inc(messages_ready[n], 1)

            walk(dve, EG, SLOTS, 7, lambda e, drain: dve_edges(1, e, drain), 1, 1)

            def middle1(p):
                b = p.slot % 2
                dve.wait_ge(product_done[1], p.g + 1)
                dve.wait_ge(scaled_ready[1], p.g + 1)
                if past(p.g, 2):
                    dve.wait_ge(hidden_turned, p.g - 1)
                dve.tensor_tensor(rows_mid[:, b, :, :], tiled(product[b]), rows_scaled[:, b, :, :], ALU.add)\
                    .then_inc(mid_ready[1], 1)

            def total1(r):
                dve.wait_ge(update_done, r.g + 1)
                dve.wait_ge(pool_ready[1], r.g + 1)
                return dve.tensor_tensor(rows_sum[:, r.slot, :, :], tiled(update[r.slot % 2]), rows_pool[:, r.slot, :, :], ALU.add)

            layer_step(1, middle1, total1, 2)

            layer_step(2, None, None, 0)

            def total3(r):
                dve.wait_ge(sums_done[3], r.g + 1)
                rows_here(dve, 3, r)
                return dve.scalar_tensor_tensor(rows_sum[:, r.slot, :, :], summed[r.slot % SUM_BANKS[3]], 0.0, rows_in[:, r.slot, :, :],
                                                ALU.max, ALU.add)

            side_by_side = dve.value_load(near[0:1, 0:1], min_val=0, max_val=1)
            with dve.If(side_by_side > 0):
                layer_step(3, None, total3, 0, True)
            with dve.Else():
                walk(dve, EG, SLOTS, 7, lambda e, drain: dve_edges(3, e, drain), 1, 1)
                layer_step(3, None, total3, 0)


_INS = ["x", "src", "dst", "edge_attr_128", "edge_attr_6", "L0_gnn_weight", "L0_gnn_bias", "L1_gnn_u", "L1_gnn_W1a",
        "L1_gnn_b1a", "L1_gnn_W1b", "L1_gnn_b1b", "L1_gnn_W2a", "L1_gnn_b2a", "L1_gnn_W2b", "L1_gnn_b2b",
        "L2_gnn_learned_weight", "L3_gnn_W", "L3_gnn_b", "L3_gnn_We", "L3_gnn_be"]


def kernel(**inputs):
    import numpy as np
    import concourse.bacc as bacc
    from concourse.bass_utils import run_bass_kernel_spmd

    nc = bacc.Bacc("TRN2", target_bir_lowering=False, num_devices=1)
    arrays, args = {}, []
    for name in _INS:
        a = np.ascontiguousarray(inputs[name])
        arrays[f"in_{name}"] = a
        args.append(nc.dram_tensor(f"in_{name}", a.shape, mybir.dt.from_np(a.dtype), kind="ExternalInput").ap())
    shape = tuple(inputs["x"].shape)
    args.append(nc.dram_tensor("out_rows", shape, F32, kind="ExternalOutput").ap())
    build(nc, *args)
    return run_bass_kernel_spmd(nc, [arrays], core_ids=[0]).results[0]["out_rows"]
```
